# Optimizing a Trainium2 kernel written in Bass

```python
import numpy as np
import jax
import jax.numpy as jnp

def _softmax(x, axis=-1):
    return jax.nn.softmax(x, axis=axis)

def _gelu(x):
    return jax.nn.gelu(x, approximate=True)

def _silu(x):
    return jax.nn.silu(x)

def _sigmoid(x):
    return jax.nn.sigmoid(x)

def _layernorm(x, axis=-1, eps=1e-05):
    m = jnp.mean(x, axis=axis, keepdims=True)
    v = jnp.var(x, axis=axis, keepdims=True)
    return (x - m) / jnp.sqrt(v + eps)

def _scatter_add(tgt, idx, src, axis=0):
    return tgt.at[idx].add(src)

def _segment_sum(src, seg, n):
    return jax.ops.segment_sum(src, seg, n)
kernel_name = 'mk_cond_resid_d2_seqx_r4_ec8181'

def setup_inputs(seed: int=0):
    np.random.seed(seed)
    _w = jnp.asarray

    def _rec_inputs():
        import jax
        import jax.numpy as jnp
        _rk = jax.random.key(seed)
        x = -7.109e-05 + 0.9999 * jax.random.normal(jax.random.fold_in(_rk, 1), (64, 64, 1024), jnp.float32)
        _lenS = 64 - jax.random.randint(jax.random.fold_in(_rk, 7), (64,), 0, max(1, 64 // 4) + 1, jnp.int32)
        _lenS2 = 64 - jax.random.randint(jax.random.fold_in(_rk, 8), (64,), 0, max(1, 64 // 4) + 1, jnp.int32)
        itok_B_4_50 = jax.random.randint(jax.random.fold_in(_rk, 11), (64,), 4, 51, jnp.int32)
        itok_B_0_7 = jax.random.randint(jax.random.fold_in(_rk, 12), (64,), 0, 8, jnp.int32)
        return (x, itok_B_4_50, itok_B_0_7)
    x, itok_B_4_50, itok_B_0_7 = _rec_inputs()

    def _L0_cond_setup():
        import jax, jax.numpy as jnp
        import numpy as np
        RANK = 16
        ALPHA = 16.0
        SCALING = ALPHA / RANK
        key = jax.random.key(seed)
        k1, k2, k3, k4 = jax.random.split(key, 4)
        batch, n_tok, d_in, d_out, n_adapters, rank = (8, 512, 1024, 1024, 64, RANK)
        x = jax.random.normal(k1, (batch, n_tok, d_in), dtype=jnp.float32)
        A = jax.random.normal(k2, (n_adapters, d_out, rank), dtype=jnp.float32) * 0.02
        B = jax.random.normal(k3, (n_adapters, rank, d_in), dtype=jnp.float32)
        adapter_ids = jax.random.randint(k4, (batch,), 0, n_adapters, dtype=jnp.int32)
        return {'x': x, 'A': A, 'B': B, 'adapter_ids': adapter_ids}
    _L0_cond_all = _L0_cond_setup()
    _L0_cond_in = {k: v for k, v in _L0_cond_all.items() if k in ('A', 'B')}
    del _L0_cond_all

    def _L1_cond_setup():
        import jax, jax.numpy as jnp
        import numpy as np
        TOP_K = 2
        LANG_BIAS = 5.0
        SCALING = 32.0 / 16.0
        LANGUAGE_PAD_ID = -1
        key = jax.random.key(seed)
        ks = jax.random.split(key, 6)
        B, T, D, O, E, R = (4, 512, 1024, 1024, 8, 16)
        x = jax.random.normal(ks[0], (B, T, D), dtype=jnp.float32)
        language_ids = jax.random.randint(ks[1], (B,), 0, E).astype(jnp.int64)
        W = jax.random.normal(ks[2], (O, D), dtype=jnp.float32) * (1.0 / np.sqrt(D))
        Wr = jax.random.normal(ks[3], (E, D), dtype=jnp.float32) * (1.0 / np.sqrt(D))
        A = jax.random.normal(ks[4], (E, R, D), dtype=jnp.float32) * (1.0 / np.sqrt(D))
        Bm = jax.random.normal(ks[5], (O, R), dtype=jnp.float32) * 0.0
        Bm = jnp.broadcast_to(Bm, (E, O, R)) + jax.random.normal(ks[5], (E, O, R), dtype=jnp.float32) * 0.02
        return {'x': x, 'language_ids': language_ids, 'W': W, 'Wr': Wr, 'A': A, 'B': Bm}
    _L1_cond_all = _L1_cond_setup()
    _L1_cond_in = {k: v for k, v in _L1_cond_all.items() if k in ('W', 'Wr', 'A', 'B')}
    del _L1_cond_all
    return {'x': x, 'itok_B_4_50': itok_B_4_50, 'itok_B_0_7': itok_B_0_7, 'L0_cond_A': _L0_cond_in['A'], 'L0_cond_B': _L0_cond_in['B'], 'L1_cond_W': _L1_cond_in['W'], 'L1_cond_Wr': _L1_cond_in['Wr'], 'L1_cond_A': _L1_cond_in['A'], 'L1_cond_B': _L1_cond_in['B']}

def reference(x, itok_B_4_50, itok_B_0_7, L0_cond_A, L0_cond_B, L1_cond_W, L1_cond_Wr, L1_cond_A, L1_cond_B):
    import jax
    import jax.numpy as jnp

    def _L0_cond_ref(x, A, B, adapter_ids):
        import jax, jax.numpy as jnp
        import numpy as np
        RANK = 16
        ALPHA = 16.0
        SCALING = ALPHA / RANK
        B_req = B[adapter_ids]
        A_req = A[adapter_ids]
        Bx = jnp.einsum('bni,bri->bnr', x, B_req)
        out = jnp.einsum('bnr,bor->bno', Bx, A_req)
        return out * SCALING

    def _L1_cond_ref(x, language_ids, W, Wr, A, B):
        import jax, jax.numpy as jnp
        import numpy as np
        TOP_K = 2
        LANG_BIAS = 5.0
        SCALING = 32.0 / 16.0
        LANGUAGE_PAD_ID = -1
        base = jnp.einsum('btd,od->bto', x, W)
        E = Wr.shape[0]
        logits = jnp.einsum('btd,ed->bte', x.astype(jnp.float32), Wr.astype(jnp.float32))
        expert_targets = language_ids
        valid = expert_targets >= 0
        tgt = jnp.where(valid, expert_targets, 0)
        bias = jax.nn.one_hot(tgt, E, dtype=logits.dtype) * LANG_BIAS
        bias = jnp.where(valid[:, None], bias, 0.0)
        logits = logits + bias[:, None, :]
        topw, topi = jax.lax.top_k(logits, TOP_K)
        weights = jax.nn.softmax(topw, axis=-1)
        gates = jnp.sum(jax.nn.one_hot(topi, E, dtype=weights.dtype) * weights[..., None], axis=-2)
        gates = gates.astype(x.dtype)
        h = jnp.einsum('btd,erd->bter', x, A)
        lora_out = jnp.einsum('bter,bte,eor->bto', h, gates, B)
        return base + SCALING * lora_out
    x = x + _L0_cond_ref(x, L0_cond_A, L0_cond_B, itok_B_4_50)
    x = x + _L1_cond_ref(x, itok_B_0_7, L1_cond_W, L1_cond_Wr, L1_cond_A, L1_cond_B)
    return x

_drawn_inputs = setup_inputs


def setup_inputs(seed=0):
    import zlib

    import numpy as np

    out = dict(_drawn_inputs(seed))
    spreads = {}
    factors = {}
    for name, (base, spread) in spreads.items():
        noise = np.random.default_rng([zlib.crc32(name.encode()), seed]).standard_normal(out[name].shape)
        drawn = base * np.exp(spread * noise) if base else spread * noise
        out[name] = jnp.asarray(drawn.astype(out[name].dtype))
    for name, factor in factors.items():
        out[name] = (out[name] * factor).astype(out[name].dtype)
    return out
```

```python
from contextlib import ExitStack

import concourse.bass as bass
from concourse import mybir

F32 = mybir.dt.float32
F32R = mybir.dt.float32r
I32 = mybir.dt.int32
U32 = mybir.dt.uint32
ALU = mybir.AluOpType
ACT = mybir.ActivationFunctionType
AX_X = mybir.AxisListType.X

P = 128
LANG_BIAS = 5.0
BANK = 512


def two_adapter_layers(nc, x, adapter_ids, lang_ids, l0_A, l0_B, l1_W, l1_Wr, l1_A, l1_B, out):
    NB, S, D = x.shape
    NAD, R, _ = l0_B.shape
    E = l1_Wr.shape[0]
    T = NB * S // P
    BPT = P // S
    TPG = P // (BPT * R)
    BPG = BPT * TPG
    G = T // TPG
    C = D // P
    CB = BANK // P
    HB = C // CB
    J = D // P
    ER = E * R
    NH = ER + E
    NW = D + NH
    BR = BPT * R
    assert ER == P and 4 * BR == P and T % TPG == 0 and HB == 2

    x_rows = x.rearrange("b s d -> (b s) d")
    out_rows = out.rearrange("b s d -> (b s) d")
    l0_A_rows = l0_A.rearrange("n (p j) r -> (n p) (j r)", j=J)
    l0_B_rows = l0_B.rearrange("n r d -> (n r) d")
    l1_A_rows = l1_A.rearrange("e r d -> (e r) d")

    with ExitStack() as ctx:
        def sb(name, shape, dt=F32):
            return ctx.enter_context(nc.sbuf_tensor(name, shape, dt))

        def bank(name):
            return ctx.enter_context(nc.psum_tensor(name, [P, BANK], F32))

        def sem(name):
            return ctx.enter_context(nc.semaphore(name))

        w_hi = sb("w_hi", [P, C, NW], F32R)
        w_lo = sb("w_lo", [P, C, NW], F32R)
        lb_hi = sb("lb_hi", [P, D], F32R)
        lb_lo = sb("lb_lo", [P, D], F32R)
        ident = sb("ident", [P, P])
        own_by_token = sb("own_by_token", [P, P])
        own = sb("own", [P, P])
        expert_no = sb("expert_no", [P, E])
        lang_bias = sb("lang_bias", [P, T, E])
        ahead = sb("ahead", [P, 2 * HB])
        aid = sb("aid", [1, NB], I32)
        lid = sb("lid", [P, NB], I32)
        lidf = sb("lidf", [P, T])
        w_in = sb("w_in", [P, 4, D])
        wr_in = sb("wr_in", [E, D])
        x_in = sb("x_in", [P, 2, D])
        a_in = sb("a_in", [P, 2, BPT, J * R])
        b_in = sb("b_in", [P, D])
        a_split = sb("a_split", [P, J, 4, BPT, R])
        a_t = sb("a_t", [P, D], F32R)
        b_t = sb("b_t", [P, C, TPG, 2, BR], F32R)
        xt_hi = sb("xt_hi", [P, C, P], F32R)
        xt_lo = sb("xt_lo", [P, C, P], F32R)
        bx = sb("bx", [P, BR])
        bx_split = sb("bx_split", [P, 2, 2, BR])
        bx_t = sb("bx_t", [P, P], F32R)
        x1_hi = sb("x1_hi", [P, 2, C, P], F32R)
        x1_lo = sb("x1_lo", [P, 2, C, P], F32R)
        logit = sb("logit", [P, E])
        top = sb("top", [P, 8])
        top_at = sb("top_at", [P, 8], U32)
        top_no = sb("top_no", [P, 2])
        expd = sb("expd", [P, 1])
        half_sum = sb("half_sum", [P, 1])
        weight = sb("weight", [P, 2])
        gate1 = sb("gate1", [P, E])
        gate2 = sb("gate2", [P, E])
        gate = sb("gate", [P, E])
        gated = sb("gated", [P, E, R])
        gt_hi = sb("gt_hi", [P, P], F32R)
        gt_lo = sb("gt_lo", [P, P], F32R)
        out_sb = sb("out_sb", [P, HB, BANK])

        X = [bank("x_bank0"), bank("x_bank1")]
        A = [bank("a_bank0"), bank("a_bank1")]
        O = [bank("o_bank0"), bank("o_bank1")]
        H = bank("h_bank")
        B = bank("b_bank")

        ids_in, b_loaded = map(sem, ("ids_in", "b_loaded"))
        x_loaded = [sem(f"x_loaded{k}") for k in range(2)]
        a_loaded = [sem(f"a_loaded{k}") for k in range(2)]
        w_loaded = [sem(f"w_loaded{i}") for i in range(4)]
        wr_loaded, lb_packed = map(sem, ("wr_loaded", "lb_packed"))
        zeros_set, consts_set, bias_ready, own_psum, own_ready = map(
            sem, ("zeros_set", "consts_set", "bias_ready", "own_psum", "own_ready"))
        w_psum, w_hi_ready, w_lo_ready, diag_ready = map(sem, ("w_psum", "w_hi_ready", "w_lo_ready", "diag_ready"))
        a_hi_ready, a_split_ready, at_psum, at_ready = map(
            sem, ("a_hi_ready", "a_split_ready", "at_psum", "at_ready"))
        bt_psum, bt_hi_ready, bt_ready = map(sem, ("bt_psum", "bt_hi_ready", "bt_ready"))
        xt_psum, xt_hi_ready, xt_lo_ready = map(sem, ("xt_psum", "xt_hi_ready", "xt_lo_ready"))
        bx_psum, bx_step, bxt_psum, bxt_ready = map(sem, ("bx_psum", "bx_step", "bxt_psum", "bxt_ready"))
        x1_psum, x1_hi_ready, x1_lo_ready = map(sem, ("x1_psum", "x1_hi_ready", "x1_lo_ready"))
        h_psum, gate_step, exp_ready, gt_psum, gt_ready = map(
            sem, ("h_psum", "gate_step", "exp_ready", "gt_psum", "gt_ready"))
        o_psum = sem("o_psum")
        out_ready = [sem(f"out{h}_ready") for h in range(HB)]
        out_stored = [sem(f"out{h}_stored") for h in range(HB)]

        tables_set = sem("tables_set")

        def count(t, per, plus=0):
            g, i = t
            return g * (TPG * per) + (i * per + plus)

        def slot_count(t, per):
            g, i = t
            return g * (TPG // 2 * per) + (i // 2 + 1) * per

        GATE = 11
        BX = 3

        NWB = D // P
        LB_SLOT = (NWB + 1) % 4
        LB_PACK = (NWB + 2) % 4

        def tile_loop(eng, body):
            with eng.Fori(0, G - 1) as g:
                for i in range(TPG):
                    body((g, i), False)
            for i in range(TPG):
                body((G - 1, i), i == TPG - 1)

        block = ctx.enter_context(nc.Block())

        @block.sync
        def _(sp):
            def load_x(t, slot):
                sp.dma_start(x_in[:, slot, :], x_rows[bass.ds(count(t, P), P), :]).then_inc(x_loaded[slot], 16)

            def adapter(no):
                return sp.value_load(aid[0:1, bass.ds(no, 1)], min_val=0, max_val=NAD - 1)

            def load_a(t, slot):
                for b in range(BPT):
                    rows = l0_A_rows[bass.ds(adapter(count(t, BPT, b)) * P, P), :]
                    sp.dma_start(a_in[:, slot, b, :], rows).then_inc(a_loaded[slot], 16)

            def load_b(g):
                for b in range(BPG):
                    rows = l0_B_rows[bass.ds(adapter(g * BPG + b) * R, R), :]
                    sp.dma_start(b_in[R * b:R * b + R, :], rows).then_inc(b_loaded, 16)

            sp.dma_start(aid[0:1, :], adapter_ids.rearrange("(a n) -> a n", a=1)).then_inc(ids_in, 16)
            sp.dma_start(lid[:, :], lang_ids.partition_broadcast(P)).then_inc(ids_in, 16)
            load_x((0, 0), 0)
            sp.dma_start(w_in[:, 0, :], l1_A_rows).then_inc(w_loaded[0], 16)
            sp.dma_start(wr_in[:, :], l1_Wr).then_inc(wr_loaded, 16)
            sp.wait_ge(ids_in, 32)
            load_b(0)
            load_a((0, 0), 0)
            load_a((0, 1), 1)
            load_x((0, 1), 1)

            def body(t, last):
                g, i = t
                final = isinstance(g, int) and i >= TPG - 2
                if not final:
                    sp.wait_ge(xt_psum, count(t, 2, 2))
                    load_x((g, i + 2), i % 2)
                    sp.wait_ge(a_split_ready, count(t, 2, 2))
                    load_a((g, i + 2), i % 2)
                if i == 0 and not isinstance(g, int):
                    sp.wait_ge(bt_psum, g * 2 + 2)
                    load_b(g + 1)
                for h in range(HB):
                    sp.wait_ge(out_ready[h], count(t, 1, 2))
                    sp.dma_start(out_rows[bass.ds(count(t, P), P), h * BANK:(h + 1) * BANK],
                                 out_sb[:, h, :]).then_inc(out_stored[h], 16)

            tile_loop(sp, body)
            for h in range(HB):
                sp.wait_ge(out_stored[h], 16 * T + 1)

        @block.gpsimd
        def _(pool):
            nc.gpsimd.memset(ident[:, :], 0.0).then_inc(zeros_set, 1)
            nc.gpsimd.memset(own_by_token[:, :], 0.0).then_inc(zeros_set, 1)
            for e in range(E):
                nc.gpsimd.memset(expert_no[:, e:e + 1], float(e)).then_inc(consts_set, 1)
            for h in range(HB):
                nc.gpsimd.memset(ahead[:, h:h + 1], 0.0).then_inc(out_ready[h], 1)
                nc.gpsimd.memset(ahead[:, HB + h:HB + h + 1], 0.0).then_inc(out_stored[h], 1)
            pool.wait_ge(zeros_set, 2)
            nc.gpsimd.affine_select(out=ident[:, :], in_=ident[:, :], compare_op=ALU.not_equal, fill=1.0,
                                    base=0, pattern=[[-1, P]], channel_multiplier=1).then_inc(consts_set, 1)
            for b in range(BPT):
                pool.wait_ge(consts_set, E + 1 + b)
                cols = own_by_token[S * b:S * b + S, :].rearrange("t (s b r) -> t s b r", b=BPT, r=R)[:, :, b, :]
                nc.gpsimd.memset(cols, 1.0).then_inc(consts_set, 1)

            def pack_l1_b():
                pool.wait_ge(w_loaded[LB_SLOT], 16 * ((NWB + 1) // 4 + 1))
                pool.wait_ge(w_psum, 2 * (NWB - 3 + 3))
                nc.gpsimd.tensor_copy(w_in[:, LB_PACK, :].rearrange("p (j e r) -> p e j r", j=J, e=E),
                                      w_in[:, LB_SLOT, :].rearrange("p (e j r) -> p e j r", e=E, j=J))\
                    .then_inc(lb_packed, 1)

            def a_lo_part(t):
                for b in range(BPT):
                    raw = a_in[:, t[1] % 2, b, :].rearrange("p (j r) -> p j r", r=R)
                    pool.wait_ge(a_hi_ready, count(t, BPT, b + 1))
                    for s in range(2):
                        sub = nc.gpsimd.tensor_tensor(a_split[:, :, 2 + s, b, :].bitcast(F32R), raw,
                                                      a_split[:, :, s, b, :], ALU.subtract)
                    sub.then_inc(a_split_ready, 1)

            pack_l1_b()

            def body(t, last):
                a_lo_part(t)

            tile_loop(pool, body)

        @block.tensor
        def _(pe):
            def turn(dst, src, start=True):
                k = src.shape[0]
                return pe.matmul(dst, src, ident[0:k, 0:k], start=start, stop=True, is_transpose=True,
                                 skip_group_check=True)

            def turn_chunks(src_of, banks, done):
                for h in range(HB):
                    for c in range(CB):
                        mm = turn(banks[h][:, c * P:(c + 1) * P], src_of(h * CB + c), start=(c == 0))
                    mm.then_inc(done, 1)

            def turn_x(n):
                pe.wait_ge(x_loaded[n[1] % 2], slot_count(n, 16))
                pe.wait_ge(x1_lo_ready, count(n, 2))
                turn_chunks(lambda c: x_in[:, n[1] % 2, c * P:(c + 1) * P], X, xt_psum)

            def turn_b(g):
                pe.wait_ge(b_loaded, g * (16 * BPG) + 16 * BPG)
                turn_chunks(lambda c: b_in[:, c * P:(c + 1) * P], A, bt_psum)

            def turn_a(n):
                pe.wait_ge(a_split_ready, count(n, 2, 2))
                turn_chunks(lambda c: a_split[:, c, :, :, :].rearrange("p s b r -> p (s b r)"), A, at_psum)

            def make_bx(n):
                g, i = n
                pe.wait_ge(bt_ready, (g if i < TPG else g + 1) * 2 + 2)
                pe.wait_ge(bxt_ready, count(n, 1))
                pe.wait_ge(xt_hi_ready, count(n, 2, 2))
                pe.wait_ge(xt_lo_ready, count(n, 2, 2))
                for c in range(C):
                    for k, xt in enumerate((xt_hi, xt_lo)):
                        mm = pe.matmul(B[:, 0:2 * BR], xt[:, c, :],
                                       b_t[:, c, i % TPG, :, :].rearrange("p s k -> p (s k)"),
                                       start=(c == 0 and k == 0), stop=(c == C - 1 and k == 1))
                mm.then_inc(bx_psum, 1)

            def turn_bx(n):
                pe.wait_ge(bx_step, count(n, BX, BX))
                turn(B[:, P:2 * P], bx_split[:, :, :, :].rearrange("p a s k -> p (a s k)")).then_inc(bxt_psum, 1)

            def add_l0(n):
                pe.wait_ge(bxt_ready, count(n, 1, 1))
                pe.wait_ge(at_ready, count(n, 2, 2))
                for h in range(HB):
                    for c in range(CB):
                        d = (h * CB + c) * P
                        mm = pe.matmul(X[h][:, c * P:(c + 1) * P], a_t[:, d:d + P], bx_t[:, :],
                                       start=False, stop=True, skip_group_check=True)
                    mm.then_inc(x1_psum, 1)

            def products(t):
                for c in range(C):
                    for xs, w in ((x1_hi, w_hi), (x1_hi, w_lo), (x1_lo, w_hi)):
                        yield c, xs[:, t[1] % 2, c, :], w

            def make_h(t):
                pe.wait_ge(x1_hi_ready, count(t, 2, 2))
                pe.wait_ge(x1_lo_ready, count(t, 2, 2))
                for k, (c, xs, w) in enumerate(products(t)):
                    mm = pe.matmul(H[:, 0:NH], xs, w[:, c, D:NW], start=(k == 0), stop=(k == 3 * C - 1))
                mm.then_inc(h_psum, 1)

            def make_o(t, h, lo, hi):
                if lo == 0:
                    pe.wait_ge(out_ready[h], count(t, 1, 1))
                for k, (c, xs, w) in enumerate(products(t)):
                    if lo <= k < hi:
                        pe.matmul(O[h][:, :], xs, w[:, c, h * BANK:(h + 1) * BANK], start=(k == 0), stop=False)

            def turn_gated(t):
                pe.wait_ge(gate_step, count(t, GATE, GATE))
                turn(H[:, 2 * P:3 * P], gated[:, :, :].rearrange("p e r -> p (e r)")).then_inc(gt_psum, 1)

            def add_lora(t, h):
                pe.wait_ge(gt_ready, count(t, 2, 2))
                for k, (gt, lb) in enumerate(((gt_hi, lb_hi), (gt_hi, lb_lo), (gt_lo, lb_hi))):
                    mm = pe.matmul(O[h][:, :], gt[:, :], lb[:, h * BANK:(h + 1) * BANK], start=False, stop=(k == 2))
                mm.then_inc(o_psum, 1)

            pe.wait_ge(consts_set, E + 1 + BPT)
            turn(B[:, 0:P], own_by_token[:, :]).then_inc(own_psum, 1)
            def weight_banks(k):
                return (A, O)[k % 2]

            def free_weight_banks(k):
                if k >= 2:
                    pe.wait_ge(w_lo_ready, 2 * (k - 1))

            pe.wait_ge(w_loaded[0], 16)
            turn_chunks(lambda c: w_in[:, 0, c * P:(c + 1) * P], weight_banks(0), w_psum)
            pe.wait_ge(wr_loaded, 16)
            for c in range(C):
                mm = turn(weight_banks(1)[0][:, c * E:(c + 1) * E], wr_in[:, c * P:(c + 1) * P])
            mm.then_inc(w_psum, 2)
            for ob in range(NWB):
                k = ob + 2
                free_weight_banks(k)
                pe.wait_ge(diag_ready, ob + 1)
                turn_chunks(lambda c: w_in[:, (ob + 1) % 4, c * P:(c + 1) * P], weight_banks(k), w_psum)
            k = NWB + 2
            free_weight_banks(k)
            pe.wait_ge(lb_packed, 1)
            turn_chunks(lambda j: w_in[:, LB_PACK, j * P:(j + 1) * P], weight_banks(k), w_psum)
            pe.wait_ge(w_lo_ready, 2 * (k - 1))
            pe.wait_ge(w_lo_ready, 2 * (k + 1))
            turn_b(0)
            turn_x((0, 0))
            pe.wait_ge(bt_ready, 2)
            turn_a((0, 0))
            make_bx((0, 0))
            turn_bx((0, 0))
            add_l0((0, 0))

            def body(t, last):
                g, i = t
                n = (g, i + 1)
                if not last:
                    turn_x(n)
                make_h(t)
                make_o(t, 0, 0, 8)
                if not last:
                    if i == TPG - 1:
                        pe.wait_ge(bt_ready, g * 2 + 4)
                    pe.wait_ge(at_ready, count(n, 2))
                    turn_a(n)
                    make_bx(n)
                make_o(t, 0, 8, 16)
                if not last:
                    turn_bx(n)
                turn_gated(t)
                make_o(t, 0, 16, 3 * C)
                if not last:
                    add_l0(n)
                add_lora(t, 0)
                if i == TPG - 2 and not isinstance(g, int):
                    pe.wait_ge(at_ready, count(n, 2, 2))
                    turn_b(g + 1)
                make_o(t, 1, 0, 3 * C)
                add_lora(t, 1)

            tile_loop(pe, body)

        @block.scalar
        def _(act):
            def w_dst(w, k, h):
                at = D if k == 0 else (k - 2) * P
                return w[:, h * CB:(h + 1) * CB, at:at + P]

            def bank_chunks(b):
                return b[:, :].rearrange("p (c m) -> p c m", c=CB)

            for k in range(1, 4):
                act.dma_start(w_in[:, k, :], l1_W[(k - 1) * P:k * P, :]).then_inc(w_loaded[k], 16)
            act.wait_ge(w_psum, 2)
            act.dma_start(w_in[:, 0, :], l1_W[3 * P:4 * P, :]).then_inc(w_loaded[0], 16)
            for k in range(NWB + 3):
                banks = (A, O)[k % 2]
                for h in range(HB):
                    act.wait_ge(w_psum, 2 * k + h + 1)
                    if k == 1:
                        if h == 0:
                            nc.scalar.copy(w_hi[:, :, D + ER:NW],
                                           banks[0][:, 0:C * E].rearrange("p (c e) -> p c e", e=E)).then_inc(w_hi_ready, 2)
                    elif k < NWB + 2:
                        nc.scalar.copy(w_dst(w_hi, k, h), bank_chunks(banks[h])).then_inc(w_hi_ready, 1)
                    else:
                        nc.scalar.copy(lb_hi[:, :].rearrange("k (p j) -> k j p", j=J)[:, h * CB:(h + 1) * CB, :],
                                       bank_chunks(banks[h])).then_inc(w_hi_ready, 1)
                if k >= 2:
                    nxt = k - 2 + 4
                    if nxt < NWB:
                        act.dma_start(w_in[:, (nxt + 1) % 4, :],
                                      l1_W[nxt * P:(nxt + 1) * P, :]).then_inc(w_loaded[(nxt + 1) % 4], 16)
                    elif nxt == NWB:
                        act.dma_start(w_in[:, (nxt + 1) % 4, :].rearrange("p (e f) -> p e f", e=E),
                                      l1_B.rearrange("e (p j) r -> p e (j r)", j=J)).then_inc(w_loaded[(nxt + 1) % 4], 16)

            def a_hi_part(n):
                act.wait_ge(a_loaded[n[1] % 2], slot_count(n, 16 * BPT))
                act.wait_ge(at_psum, count(n, 2))
                for b in range(BPT):
                    raw = a_in[:, n[1] % 2, b, :].rearrange("p (j r) -> p j r", r=R)
                    for s in range(2):
                        copy = nc.scalar.copy(a_split[:, :, s, b, :].bitcast(F32R), raw)
                    copy.then_inc(a_hi_ready, 1)

            def xt_hi_part(n):
                act.wait_ge(bx_psum, count(n, 1))
                for h in range(HB):
                    act.wait_ge(xt_psum, count(n, 2, h + 1))
                    nc.scalar.copy(xt_hi[:, h * CB:(h + 1) * CB, :], bank_chunks(X[h])).then_inc(xt_hi_ready, 1)

            def a_part(n):
                act.wait_ge(x1_psum, count(n, 2))
                for h in range(HB):
                    act.wait_ge(at_psum, count(n, 2, h + 1))
                    nc.scalar.copy(a_t[:, :].bitcast(F32).rearrange("k (p j) -> k j p", j=J)[:, h * CB:(h + 1) * CB, :].bitcast(F32R),
                                   bank_chunks(A[h])).then_inc(at_ready, 1)

            def x1_hi_part(n):
                for h in range(HB):
                    act.wait_ge(x1_psum, count(n, 2, h + 1))
                    nc.scalar.copy(x1_hi[:, n[1] % 2, h * CB:(h + 1) * CB, :], bank_chunks(X[h])).then_inc(x1_hi_ready, 1)

            def exp_part(t):
                act.wait_ge(gate_step, count(t, GATE, 2))
                nc.scalar.activation(expd[:, :], top[:, 0:1], ACT.Exp, bias=top[:, 1:2],
                                     scale=-1.0).then_inc(exp_ready, 1)

            def out_part(t, h):
                act.wait_ge(out_stored[h], count(t, 16, 1))
                act.wait_ge(o_psum, count(t, HB, h + 1))
                nc.scalar.copy(out_sb[:, h, :], O[h][:, :]).then_inc(out_ready[h], 1)

            a_hi_part((0, 0))
            xt_hi_part((0, 0))
            a_part((0, 0))
            x1_hi_part((0, 0))
            a_hi_part((0, 1))

            def body(t, last):
                n = (t[0], t[1] + 1)
                if not last:
                    xt_hi_part(n)
                exp_part(t)
                if not last:
                    a_part(n)
                    x1_hi_part(n)
                out_part(t, 0)
                if not (isinstance(t[0], int) and t[1] >= TPG - 2):
                    a_hi_part((t[0], t[1] + 2))
                out_part(t, 1)

            tile_loop(act, body)

        @block.vector
        def _(dve):
            def bank_chunks(b):
                return b[:, :].rearrange("p (c m) -> p c m", c=CB)

            def minus(dst, psum, hi):
                return nc.vector.tensor_tensor(dst, psum, hi.bitcast(F32), ALU.subtract)

            dve.wait_ge(ids_in, 32)
            for b in range(BPT):
                nc.vector.tensor_copy(lidf[S * b:S * b + S, :],
                                      lid[S * b:S * b + S, :].rearrange("p (t b) -> p t b", b=BPT)[:, :, b])\
                    .then_inc(bias_ready, 1)
            dve.wait_ge(consts_set, E + 1 + BPT)
            dve.wait_ge(bias_ready, BPT)
            nc.vector.tensor_tensor(lang_bias[:, :, :], lidf[:, :].unsqueeze(2).to_broadcast([P, T, E]),
                                    expert_no[:, :].unsqueeze(1).to_broadcast([P, T, E]),
                                    ALU.is_equal).then_inc(bias_ready, 1)
            dve.wait_ge(bias_ready, BPT + 1)
            nc.vector.tensor_scalar(lang_bias[:, :, :], lang_bias[:, :, :], LANG_BIAS, None,
                                    ALU.mult).then_inc(tables_set, 1)
            dve.wait_ge(own_psum, 1)
            nc.vector.tensor_copy(own[:, :], B[:, 0:P]).then_inc(own_ready, 1)

            def add_identity(ob):
                slot = (ob + 1) % 4
                dve.wait_ge(w_loaded[slot], 16 * ((ob + 1) // 4 + 1))
                diag = w_in[:, slot, ob * P:(ob + 1) * P]
                nc.vector.tensor_tensor(diag, diag, ident[:, :], ALU.add).then_inc(diag_ready, 1)

            for ob in range(2):
                add_identity(ob)
            for k in range(NWB + 3):
                banks = (A, O)[k % 2]
                at = D if k == 0 else (k - 2) * P
                for h in range(HB):
                    dve.wait_ge(w_hi_ready, 2 * k + h + 1)
                    if k == 1:
                        if h == 0:
                            minus(w_lo[:, :, D + ER:NW], banks[0][:, 0:C * E].rearrange("p (c e) -> p c e", e=E),
                                  w_hi[:, :, D + ER:NW]).then_inc(w_lo_ready, 2)
                    elif k < NWB + 2:
                        cols = (slice(None), slice(h * CB, (h + 1) * CB), slice(at, at + P))
                        minus(w_lo[cols], bank_chunks(banks[h]), w_hi[cols]).then_inc(w_lo_ready, 1)
                    else:
                        cols = (slice(None), slice(h * CB, (h + 1) * CB), slice(None))
                        minus(lb_lo[:, :].rearrange("k (p j) -> k j p", j=J)[cols], bank_chunks(banks[h]),
                              lb_hi[:, :].rearrange("k (p j) -> k j p", j=J)[cols]).then_inc(w_lo_ready, 1)
                if 2 <= k + 2 < NWB:
                    add_identity(k + 2)

            def xt_lo_part(n, h):
                dve.wait_ge(xt_hi_ready, count(n, 2, h + 1))
                cols = (slice(None), slice(h * CB, (h + 1) * CB), slice(None))
                minus(xt_lo[cols], bank_chunks(X[h]), xt_hi[cols]).then_inc(xt_lo_ready, 1)

            def b_part(g):
                for h in range(HB):
                    src = A[h][:, :].rearrange("p (c t k) -> p c t k", c=CB, t=TPG)
                    dve.wait_ge(bt_psum, g * 2 + (h + 1))
                    nc.vector.tensor_copy(b_t[:, h * CB:(h + 1) * CB, :, 0, :], src).then_inc(bt_hi_ready, 1)
                    dve.wait_ge(bt_hi_ready, g * 2 + (h + 1))
                    minus(b_t[:, h * CB:(h + 1) * CB, :, 1, :], src,
                          b_t[:, h * CB:(h + 1) * CB, :, 0, :]).then_inc(bt_ready, 1)

            def bx_part(n):
                dve.wait_ge(bx_psum, count(n, 1, 1))
                nc.vector.tensor_reduce(bx[:, :], B[:, 0:2 * BR].rearrange("p (s k) -> p k s", s=2), AX_X,
                                        ALU.add).then_inc(bx_step, 1)
                dve.wait_ge(bx_step, count(n, BX, 1))
                dve.wait_ge(bxt_psum, count(n, 1))
                twice = bx[:, :].unsqueeze(1).to_broadcast([P, 2, BR])
                nc.vector.tensor_copy(bx_split[:, :, 0, :].bitcast(F32R), twice).then_inc(bx_step, 1)
                dve.wait_ge(bx_step, count(n, BX, 2))
                nc.vector.tensor_tensor(bx_split[:, :, 1, :].bitcast(F32R), twice, bx_split[:, :, 0, :],
                                        ALU.subtract).then_inc(bx_step, 1)

            def bxt_part(n):
                dve.wait_ge(x1_psum, count(n, 2))
                dve.wait_ge(bxt_psum, count(n, 1, 1))
                nc.vector.tensor_tensor(bx_t[:, :], B[:, P:2 * P], own[:, :], ALU.mult).then_inc(bxt_ready, 1)

            def x1_lo_part(n):
                for h in range(HB):
                    dve.wait_ge(x1_hi_ready, count(n, 2, h + 1))
                    psum, src = X[h], x1_hi[:, n[1] % 2, h * CB:(h + 1) * CB, :]
                    minus(x1_lo[:, n[1] % 2, h * CB:(h + 1) * CB, :], bank_chunks(psum), src).then_inc(x1_lo_ready, 1)

            def gating(t, n, last):
                def after(k):
                    dve.wait_ge(gate_step, count(t, GATE, k))

                dve.wait_ge(h_psum, count(t, 1, 1))
                tile_bias = lang_bias[:, bass.ds(count(t, 1), 1), :].rearrange("p a e -> p (a e)")
                nc.vector.tensor_tensor(logit[:, :], H[:, ER:NH], tile_bias, ALU.add).then_inc(gate_step, 1)
                after(1)
                if not last:
                    xt_lo_part(n, 0)
                nc.vector.max(top[:, :], logit[:, :]).then_inc(gate_step, 1)
                after(2)
                if not last:
                    xt_lo_part(n, 1)
                nc.vector.max_index(top_at[:, :], top[:, :], logit[:, :]).then_inc(gate_step, 1)
                after(3)
                nc.vector.tensor_copy(top_no[:, :], top_at[:, 0:2]).then_inc(gate_step, 1)
                dve.wait_ge(exp_ready, count(t, 1, 1))
                nc.vector.tensor_scalar(half_sum[:, :], expd[:, :], 1.0, 0.5, ALU.add, ALU.mult).then_inc(gate_step, 1)
                after(5)
                nc.vector.reciprocal(weight[:, 0:1], half_sum[:, :]).then_inc(gate_step, 1)
                after(6)
                nc.vector.tensor_tensor(weight[:, 1:2], weight[:, 0:1], expd[:, :], ALU.mult).then_inc(gate_step, 1)
                after(7)
                nc.vector.tensor_scalar(gate1[:, :], expert_no[:, :], top_no[:, 0:1], weight[:, 0:1],
                                        ALU.is_equal, ALU.mult).then_inc(gate_step, 1)
                nc.vector.tensor_scalar(gate2[:, :], expert_no[:, :], top_no[:, 1:2], weight[:, 1:2],
                                        ALU.is_equal, ALU.mult).then_inc(gate_step, 1)
                after(9)
                nc.vector.tensor_tensor(gate[:, :], gate1[:, :], gate2[:, :], ALU.add).then_inc(gate_step, 1)
                after(10)
                nc.vector.tensor_tensor(gated[:, :, :], H[:, 0:ER].rearrange("p (e r) -> p e r", r=R),
                                        gate[:, :].unsqueeze(2).to_broadcast([P, E, R]),
                                        ALU.mult).then_inc(gate_step, 1)

            def gated_t_part(t):
                dve.wait_ge(gt_psum, count(t, 1, 1))
                nc.vector.tensor_copy(gt_hi[:, :], H[:, 2 * P:3 * P]).then_inc(gt_ready, 1)
                dve.wait_ge(gt_ready, count(t, 2, 1))
                minus(gt_lo[:, :], H[:, 2 * P:3 * P], gt_hi[:, :]).then_inc(gt_ready, 1)

            dve.wait_ge(tables_set, 1)
            dve.wait_ge(own_ready, 1)
            b_part(0)
            xt_lo_part((0, 0), 0)
            xt_lo_part((0, 0), 1)
            bx_part((0, 0))
            bxt_part((0, 0))
            x1_lo_part((0, 0))

            def body(t, last):
                g, i = t
                n = (g, i + 1)
                gating(t, n, last)
                if not last:
                    bx_part(n)
                    bxt_part(n)
                gated_t_part(t)
                if not last:
                    x1_lo_part(n)
                if i == TPG - 2 and not isinstance(g, int):
                    b_part(g + 1)

            tile_loop(dve, body)


_INS = ["x", "itok_B_4_50", "itok_B_0_7", "L0_cond_A", "L0_cond_B", "L1_cond_W", "L1_cond_Wr", "L1_cond_A", "L1_cond_B"]


def kernel(**inputs):
    import numpy as _np
    import concourse.bacc as _bacc
    from concourse import mybir as _mybir
    from concourse.bass_utils import run_bass_kernel_spmd as _run

    nc = _bacc.Bacc("TRN2", target_bir_lowering=False, num_devices=1)
    arrays, args = {}, []
    for name in _INS:
        a = _np.ascontiguousarray(inputs[name])
        arrays[f"in_{name}_dram"] = a
        args.append(nc.dram_tensor(f"in_{name}_dram", a.shape, _mybir.dt.from_np(a.dtype), kind="ExternalInput").ap())
    shape = inputs["x"].shape
    args.append(nc.dram_tensor("out_0_dram", shape, _mybir.dt.float32, kind="ExternalOutput").ap())
    two_adapter_layers(nc, *args)
    r = _run(nc, [arrays], core_ids=[0])
    return r.results[0]["out_0_dram"]
```

```python
from contextlib import ExitStack

import concourse.bass as bass
from concourse import mybir

F32 = mybir.dt.float32
F32R = mybir.dt.float32r
I32 = mybir.dt.int32
U32 = mybir.dt.uint32
ALU = mybir.AluOpType
ACT = mybir.ActivationFunctionType

P = 128
LANG_BIAS = 5.0
BANK = 512


def two_adapter_layers(nc, x, adapter_ids, lang_ids, l0_A, l0_B, l1_W, l1_Wr, l1_A, l1_B, out):
    NB, S, D = x.shape
    NAD, R, _ = l0_B.shape
    E = l1_Wr.shape[0]
    T = NB * S // P
    BPT = P // S
    BR = BPT * R
    TPG = P // BR
    PPG = TPG // 2
    BPG = BPT * TPG
    G = T // TPG
    C = D // P
    CB = BANK // P
    HB = C // CB
    J = D // P
    ER = E * R
    NH = ER + E
    NW = NH + D
    REST = (NW - BANK) // 2
    PARTS = [(0, BANK), (BANK, BANK + REST), (BANK + REST, NW)]
    NP = len(PARTS)
    K3 = 3 * C
    Q = P // 2
    assert ER == P and 4 * BR == P and TPG == 4 and T % TPG == 0 and HB == 2 and REST % 2 == 0

    x_rows = x.rearrange("b s d -> (b s) d")
    out_rows = out.rearrange("b s d -> (b s) d")
    l0_A_rows = l0_A.rearrange("n (p j) r -> (n p) (j r)", j=J)
    l0_B_rows = l0_B.rearrange("n r d -> (n r) d")
    l1_A_rows = l1_A.rearrange("e r d -> (e r) d")

    NWB = D // P
    SLOTS = 8
    BLOCK_A, BLOCK_B = 0, NWB + 1
    LB_PACK = (BLOCK_B + 1) % SLOTS
    BATCHES = NWB + 3
    B_WR, B_LB = 1, NWB + 2
    ON_A = (0, 2, 4, 9)
    BEFORE = {2: 0, 3: 1, 4: 2, 5: 3, 6: 5, 7: 6, 8: 7}

    with ExitStack() as ctx:
        def sb(name, shape, dt=F32):
            return ctx.enter_context(nc.sbuf_tensor(name, shape, dt))

        def bank(name):
            return ctx.enter_context(nc.psum_tensor(name, [P, BANK], F32))

        def sem(name):
            return ctx.enter_context(nc.semaphore(name))

        w_hi = sb("w_hi", [P, C, NW], F32R)
        w_lo = sb("w_lo", [P, C, NW], F32R)
        lb_hi = sb("lb_hi", [P, D], F32R)
        lb_lo = sb("lb_lo", [P, D], F32R)
        ident = sb("ident", [P, P])
        own_by_token = sb("own_by_token", [P, P])
        own = sb("own", [P, P])
        expert_no = sb("expert_no", [P, E])
        lang_bias = sb("lang_bias", [P, T, E])
        ahead = sb("ahead", [P, NP + 1])
        aid = sb("aid", [1, NB], I32)
        lid = sb("lid", [P, NB], I32)
        lidf = sb("lidf", [P, T])
        w_in = sb("w_in", [P, SLOTS, D])
        wr_in = sb("wr_in", [E, D])
        x_in = sb("x_in", [P, 2, D])
        a_in = sb("a_in", [P, 2, BPT, J * R])
        b_in = sb("b_in", [P, D])
        a_split = sb("a_split", [P, J, 2, 2, BPT, R])
        a_t = sb("a_t", [P, 2, D], F32R)
        b_t = sb("b_t", [P, C, TPG, 2, 2, BR], F32R)
        xt = sb("xt", [P, C, 2, P], F32R)
        swap = sb("swap", [P, 2, P])
        bx_sum = sb("bx_sum", [P, 2, P])
        bx_all = sb("bx_all", [P, P])
        bx_own = sb("bx_own", [P, P])
        bx_hi = sb("bx_hi", [P, P])
        bx_t = sb("bx_t", [P, P], F32R)
        x1_hi = sb("x1_hi", [P, 2, C, P], F32R)
        x1_lo = sb("x1_lo", [P, 2, C, P], F32R)
        logit = sb("logit", [P, E])
        top = sb("top", [P, 8])
        top_at = sb("top_at", [P, 8], U32)
        top_no = sb("top_no", [P, 2])
        expd = sb("expd", [P, 1])
        half_sum = sb("half_sum", [P, 1])
        weight = sb("weight", [P, 2])
        gate1 = sb("gate1", [P, E])
        gate2 = sb("gate2", [P, E])
        gate = sb("gate", [P, E])
        gated = sb("gated", [P, E, R])
        gt_hi = sb("gt_hi", [P, P], F32R)
        gt_lo = sb("gt_lo", [P, P], F32R)
        out_sb = sb("out_sb", [P, D])

        X = [bank("x_bank0"), bank("x_bank1")]
        A = [bank("a_bank0"), bank("a_bank1")]
        O = [bank("o_bank0"), bank("o_bank1"), bank("o_bank2")]
        B = bank("b_bank")
        SPARE = [O[2], B]

        aid_in, lid_in, wr_loaded, b_loaded = map(sem, ("aid_in", "lid_in", "wr_loaded", "b_loaded"))
        a_first_loaded, a_loaded = map(sem, ("a_first_loaded", "a_loaded"))
        x_loaded = [sem(f"x_loaded{k}") for k in range(2)]
        w_loaded = [sem(f"w_loaded{k}") for k in range(SLOTS)]
        zeros_set, consts_set, lid_ready, tables_set, own_psum, own_ready = map(
            sem, ("zeros_set", "consts_set", "lid_ready", "tables_set", "own_psum", "own_ready"))
        diag_ready, w_psum, w_hi_ready, w_lo_ready, lb_packed = map(
            sem, ("diag_ready", "w_psum", "w_hi_ready", "w_lo_ready", "lb_packed"))
        a_hi_ready, a_split_ready, at_psum, at_ready = map(
            sem, ("a_hi_ready", "a_split_ready", "at_psum", "at_ready"))
        bt_psum, bt_hi_ready, bt_ready = map(sem, ("bt_psum", "bt_hi_ready", "bt_ready"))
        xt_psum, xt_hi_ready, xt_lo_ready = map(sem, ("xt_psum", "xt_hi_ready", "xt_lo_ready"))
        bx_psum, swap_ready, bx_step = map(sem, ("bx_psum", "swap_ready", "bx_step"))
        x1_psum, x1_hi_ready, x1_lo_ready = map(sem, ("x1_psum", "x1_hi_ready", "x1_lo_ready"))
        h_psum, gate_step, exp_ready, gt_psum, gt_ready = map(
            sem, ("h_psum", "gate_step", "exp_ready", "gt_psum", "gt_ready"))
        o_psum, out_stored = map(sem, ("o_psum", "out_stored"))
        out_ready = [sem(f"out{k}_ready") for k in range(NP)]

        def count(t, per, plus=0):
            g, i = t
            return g * (TPG * per) + (i * per + plus)

        def pair_count(p, per, plus=0):
            g, q = p
            return g * (PPG * per) + (q * per + plus)

        def slot_count(t, per):
            g, i = t
            return g * (PPG * per) + (i // 2 + 1) * per

        FIRST = (0, 0)
        GATE = 11
        BX = 6
        AT = 8

        def tile_loop(eng, body):
            with eng.Fori(0, G - 1) as g:
                for i in range(TPG):
                    body((g, i), False, False)
            for i in range(TPG):
                body((G - 1, i), True, i == TPG - 1)

        def weight_banks(k):
            return SPARE if k == B_LB else A if k in ON_A else O[0:HB]

        def weight_cols(k):
            return slice(0, ER) if k == 0 else slice(NH + (k - 2) * P, NH + (k - 1) * P)

        def bank_chunks(b):
            return b[:, :].rearrange("p (c m) -> p c m", c=CB)

        def by_j(row):
            return row.rearrange("k (p j) -> k j p", j=J)

        def b_views(h, banks):
            src = banks[h][:, :].rearrange("p (m k) -> p m k", k=BR).unsqueeze(2).to_broadcast([P, CB * TPG, 2, BR])
            dst = b_t[:, h * CB:(h + 1) * CB, :, :, :, :].rearrange("p c t s a k -> p (c t) s a k")
            return src, dst

        block = ctx.enter_context(nc.Block())

        @block.sync
        def _(sp):
            def load_x(t, slot):
                sp.dma_start(x_in[:, slot, :], x_rows[bass.ds(count(t, P), P), :]).then_inc(x_loaded[slot], 16)

            def adapter(no):
                return sp.value_load(aid[0:1, bass.ds(no, 1)], min_val=0, max_val=NAD - 1)

            def load_a(p):
                for b in range(2 * BPT):
                    rows = l0_A_rows[bass.ds(adapter(pair_count(p, 2 * BPT, b)) * P, P), :]
                    sp.dma_start(a_in[:, b // BPT, b % BPT, :], rows).then_inc(a_loaded, 16)

            def load_b(g):
                for b in range(BPG):
                    rows = l0_B_rows[bass.ds(adapter(g * BPG + b) * R, R), :]
                    sp.dma_start(b_in[R * b:R * b + R, :], rows).then_inc(b_loaded, 16)

            sp.dma_start(aid[0:1, :], adapter_ids.rearrange("(a n) -> a n", a=1)).then_inc(aid_in, 16)
            load_x((0, 0), 0)
            sp.dma_start(lid[:, :], lang_ids.partition_broadcast(P)).then_inc(lid_in, 16)
            sp.wait_ge(aid_in, 16)
            load_b(0)
            load_x((0, 1), 1)
            sp.wait_ge(a_split_ready, 2 * BPT)
            load_a((0, 1))

            def body(t, last_group, last):
                g, i = t
                if not (last_group and i >= TPG - 2):
                    sp.wait_ge(xt_psum, count(t, HB, HB))
                    load_x((g, i + 2), i % 2)
                if not last_group and i % 2 == 1:
                    p = (g, i // 2 + 1)
                    sp.wait_ge(a_split_ready, pair_count(p, 2 * BPT, 2 * BPT))
                    load_a((g, i // 2 + 2))
                if not last_group and i == 0:
                    sp.wait_ge(bt_psum, g * HB + HB)
                    load_b(g + 1)
                for k in range(NP):
                    sp.wait_ge(out_ready[k], count(t, 1, 2))
                sp.dma_start(out_rows[bass.ds(count(t, P), P), :], out_sb[:, :]).then_inc(out_stored, 16)

            tile_loop(sp, body)
            sp.wait_ge(out_stored, 16 * T + 1)

        @block.gpsimd
        def _(pool):
            nc.gpsimd.memset(ident[:, :], 0.0).then_inc(zeros_set, 1)
            nc.gpsimd.memset(own_by_token[:, :], 0.0).then_inc(zeros_set, 1)
            for e in range(E):
                nc.gpsimd.memset(expert_no[:, e:e + 1], float(e)).then_inc(consts_set, 1)
            for k in range(NP):
                nc.gpsimd.memset(ahead[:, k:k + 1], 0.0).then_inc(out_ready[k], 1)
            nc.gpsimd.memset(ahead[:, NP:NP + 1], 0.0).then_inc(out_stored, 1)
            pool.wait_ge(zeros_set, 2)
            nc.gpsimd.affine_select(out=ident[:, :], in_=ident[:, :], compare_op=ALU.not_equal, fill=1.0,
                                    base=0, pattern=[[-1, P]], channel_multiplier=1).then_inc(consts_set, 1)
            for b in range(BPT):
                pool.wait_ge(consts_set, E + 1 + b)
                cols = own_by_token[S * b:S * b + S, :].rearrange("t (s b r) -> t s b r", b=BPT, r=R)[:, :, b, :]
                nc.gpsimd.memset(cols, 1.0).then_inc(consts_set, 1)

            pool.wait_ge(aid_in, 16)
            for b in range(2 * BPT):
                no = pool.value_load(aid[0:1, b:b + 1], min_val=0, max_val=NAD - 1)
                pool.dma_start(a_in[:, b // BPT, b % BPT, :],
                               l0_A_rows[bass.ds(no * P, P), :]).then_inc(a_first_loaded, 16)

            def add_identity(m):
                pool.wait_ge(w_loaded[m % SLOTS], 16 * (m // SLOTS + 1))
                diag = w_in[:, m % SLOTS, (m - 1) * P:m * P]
                nc.gpsimd.tensor_tensor(diag, diag, ident[:, :], ALU.add).then_inc(diag_ready, 1)

            def a_lo_part(p):
                for b in range(2 * BPT):
                    k, b1 = b // BPT, b % BPT
                    raw = a_in[:, k, b1, :].rearrange("p (j r) -> p j r", r=R)
                    pool.wait_ge(a_hi_ready, pair_count(p, 2 * BPT, b + 1))
                    nc.gpsimd.tensor_tensor(a_split[:, :, k, 1, b1, :].bitcast(F32R), raw,
                                            a_split[:, :, k, 0, b1, :], ALU.subtract).then_inc(a_split_ready, 1)

            pool.wait_ge(consts_set, E + 1 + BPT)
            for m in range(1, 4):
                add_identity(m)
            a_lo_part((0, 0))
            for m in range(4, NWB + 1):
                add_identity(m)
            pool.wait_ge(w_loaded[BLOCK_B % SLOTS], 16 * (BLOCK_B // SLOTS + 1))
            pool.wait_ge(w_psum, HB * (LB_PACK + 2))
            nc.gpsimd.tensor_copy(w_in[:, LB_PACK, :].rearrange("p (j e r) -> p e j r", j=J, e=E),
                                  w_in[:, BLOCK_B % SLOTS, :].rearrange("p (e j r) -> p e j r", e=E, j=J))\
                .then_inc(lb_packed, 1)

            def body(t, last_group, last):
                g, i = t
                if i % 2 == 0 and not (last_group and i == TPG - 2):
                    a_lo_part((g, i // 2 + 1))

            tile_loop(pool, body)

        @block.tensor
        def _(pe):
            def turn(dst, src, start=True):
                k = src.shape[0]
                return pe.matmul(dst, src, ident[0:k, 0:k], start=start, stop=True, is_transpose=True,
                                 skip_group_check=True)

            def turn_chunks(src_of, banks, done):
                for h in range(HB):
                    for c in range(CB):
                        mm = turn(banks[h][:, c * P:(c + 1) * P], src_of(h * CB + c), start=(c == 0))
                    mm.then_inc(done, 1)

            def turn_x(n):
                pe.wait_ge(x_loaded[n[1] % 2], slot_count(n, 16))
                if n is not FIRST:
                    pe.wait_ge(x1_lo_ready, count(n, HB))
                turn_chunks(lambda c: x_in[:, n[1] % 2, c * P:(c + 1) * P], X, xt_psum)

            def turn_b(g, banks=A):
                pe.wait_ge(b_loaded, g * (16 * BPG) + 16 * BPG)
                turn_chunks(lambda c: b_in[:, c * P:(c + 1) * P], banks, bt_psum)

            def turn_a(p):
                pe.wait_ge(a_split_ready, pair_count(p, 2 * BPT, 2 * BPT))
                turn_chunks(lambda c: a_split[:, c, :, :, :, :].rearrange("p k w b r -> p (k w b r)"), A, at_psum)

            def make_bx(n):
                g, i = n
                pe.wait_ge(bt_ready, (g + i // TPG) * HB + HB)
                if n is not FIRST:
                    pe.wait_ge(w_lo_ready, HB * BATCHES)
                pe.wait_ge(xt_hi_ready, count(n, HB, HB))
                pe.wait_ge(xt_lo_ready, count(n, HB, HB))
                for c in range(C):
                    mm = pe.matmul(B[:, 0:2 * P], b_t[:, c, i % TPG, :, :, :].rearrange("p s a k -> p (s a k)"),
                                   xt[:, c, :, :].rearrange("p u t -> p (u t)"), start=(c == 0), stop=(c == C - 1))
                mm.then_inc(bx_psum, 1)

            def add_l0(n):
                g, i = n
                k = i % 2
                pe.wait_ge(bx_step, count(n, BX, BX))
                pe.wait_ge(at_ready, pair_count((g, i // 2), AT, AT // 2 * (k + 1)))
                for h in range(HB):
                    for c in range(CB):
                        d = (h * CB + c) * P
                        mm = pe.matmul(X[h][:, c * P:(c + 1) * P], a_t[:, k, d:d + P], bx_t[:, :],
                                       start=False, stop=True, skip_group_check=True)
                    mm.then_inc(x1_psum, 1)

            def make_part(t, part, first, end):
                lo, hi = PARTS[part]
                if first == 0:
                    pe.wait_ge(w_lo_ready, HB * (B_LB - 1 if part < NP - 1 else BATCHES))
                    pe.wait_ge(out_ready[part], count(t, 1, 1))
                for k in range(first, end):
                    c = k // 3
                    xs, w = ((x1_hi, w_hi), (x1_hi, w_lo), (x1_lo, w_hi))[k % 3]
                    mm = pe.matmul(O[part][:, 0:hi - lo], xs[:, t[1] % 2, c, :], w[:, c, lo:hi],
                                   start=(k == 0), stop=(k == K3 - 1), skip_group_check=True)
                return mm

            def turn_gated(t):
                pe.wait_ge(gate_step, count(t, GATE, GATE))
                turn(B[:, 2 * P:3 * P], gated[:, :, :].rearrange("p e r -> p (e r)")).then_inc(gt_psum, 1)

            def add_lora(part):
                lo, hi = PARTS[part]
                skip = NH if part == 0 else 0
                for k, (gt, lb) in enumerate(((gt_hi, lb_hi), (gt_hi, lb_lo), (gt_lo, lb_hi))):
                    mm = pe.matmul(O[part][:, skip:hi - lo], gt[:, :], lb[:, lo + skip - NH:hi - NH],
                                   start=False, stop=(k == 2), skip_group_check=True)
                mm.then_inc(o_psum, 1)

            def turn_weights(k):
                if k in BEFORE:
                    pe.wait_ge(w_lo_ready, HB * (BEFORE[k] + 1))
                if k == 9:
                    pe.wait_ge(at_ready, AT)
                if k == B_WR:
                    pe.wait_ge(wr_loaded, 16)
                    for c in range(C):
                        mm = turn(weight_banks(k)[0][:, c * E:(c + 1) * E], wr_in[:, c * P:(c + 1) * P])
                    mm.then_inc(w_psum, HB)
                    return
                if k == 0:
                    pe.wait_ge(w_loaded[0], 16)
                    slot = 0
                elif k == B_LB:
                    pe.wait_ge(lb_packed, 1)
                    slot = LB_PACK
                else:
                    pe.wait_ge(diag_ready, k - 1)
                    slot = (k - 1) % SLOTS
                turn_chunks(lambda c: w_in[:, slot, c * P:(c + 1) * P], weight_banks(k), w_psum)

            pe.wait_ge(consts_set, E + 1 + BPT)
            turn(B[:, 0:P], own_by_token[:, :]).then_inc(own_psum, 1)
            turn_weights(0)
            turn_x(FIRST)
            for k in range(1, 6):
                turn_weights(k)
            pe.wait_ge(own_ready, 1)
            turn_b(0, SPARE)
            pe.wait_ge(w_lo_ready, HB * 5)
            turn_a(FIRST)
            turn_weights(6)
            make_bx(FIRST)
            turn_weights(7)
            add_l0((0, 0))
            turn_weights(8)
            turn_weights(9)
            turn_weights(10)

            def body(t, last_group, last):
                g, i = t
                n = (g, i + 1)
                if not last:
                    turn_x(n)
                pe.wait_ge(x1_hi_ready, count(t, HB, HB))
                pe.wait_ge(x1_lo_ready, count(t, HB, HB))
                if not last:
                    make_part(t, 0, 0, 9)
                    if i % 2 == 1:
                        p = (g, i // 2 + 1)
                        if i == TPG - 1:
                            pe.wait_ge(bt_ready, g * HB + 2 * HB)
                        else:
                            pe.wait_ge(at_ready, pair_count(p, AT))
                        turn_a(p)
                    make_part(t, 0, 9, 18)
                    make_bx(n)
                    make_part(t, 0, 18, K3).then_inc(h_psum, 1)
                else:
                    make_part(t, 0, 0, K3).then_inc(h_psum, 1)
                if i == TPG - 2 and not last_group:
                    pe.wait_ge(at_ready, pair_count((g, 1), AT, AT))
                    turn_b(g + 1)
                make_part(t, 1, 0, 21)
                if not last:
                    add_l0(n)
                make_part(t, 1, 21, K3)
                turn_gated(t)
                make_part(t, 2, 0, 12)
                pe.wait_ge(gt_ready, count(t, 2, 2))
                add_lora(0)
                add_lora(1)
                make_part(t, 2, 12, K3)
                add_lora(2)

            tile_loop(pe, body)

        @block.scalar
        def _(act):
            def load_block(m):
                slot = m % SLOTS
                if m == BLOCK_A:
                    act.dma_start(w_in[:, slot, :], l1_A_rows).then_inc(w_loaded[slot], 16)
                elif m == BLOCK_B:
                    act.dma_start(w_in[:, slot, :].rearrange("p (e f) -> p e f", e=E),
                                  l1_B.rearrange("e (p j) r -> p e (j r)", j=J)).then_inc(w_loaded[slot], 16)
                else:
                    act.dma_start(w_in[:, slot, :], l1_W[(m - 1) * P:m * P, :]).then_inc(w_loaded[slot], 16)

            def w_hi_part(k):
                banks = weight_banks(k)
                if k == B_WR:
                    act.wait_ge(w_psum, HB * k + HB)
                    nc.scalar.copy(w_hi[:, :, ER:NH],
                                   banks[0][:, 0:C * E].rearrange("p (c e) -> p c e", e=E)).then_inc(w_hi_ready, HB)
                    return
                for h in range(HB):
                    chunks = slice(h * CB, (h + 1) * CB)
                    dst = by_j(lb_hi[:, :])[:, chunks, :] if k == B_LB else w_hi[:, chunks, weight_cols(k)]
                    act.wait_ge(w_psum, HB * k + h + 1)
                    nc.scalar.copy(dst, bank_chunks(banks[h])).then_inc(w_hi_ready, 1)

            def a_hi_part(p):
                if p is FIRST:
                    act.wait_ge(a_first_loaded, 32 * BPT)
                else:
                    act.wait_ge(a_loaded, pair_count(p, 32 * BPT))
                    act.wait_ge(at_psum, pair_count(p, HB))
                for b in range(2 * BPT):
                    k, b1 = b // BPT, b % BPT
                    nc.scalar.copy(a_split[:, :, k, 0, b1, :].bitcast(F32R),
                                   a_in[:, k, b1, :].rearrange("p (j r) -> p j r", r=R)).then_inc(a_hi_ready, 1)

            def xt_hi_part(n):
                if n is not FIRST:
                    act.wait_ge(bx_psum, count(n, 1))
                for h in range(HB):
                    act.wait_ge(xt_psum, count(n, HB, h + 1))
                    nc.scalar.copy(xt[:, h * CB:(h + 1) * CB, 0, :], bank_chunks(X[h])).then_inc(xt_hi_ready, 1)

            def a_part(p, k):
                if p is not FIRST:
                    act.wait_ge(x1_psum, pair_count(p, 2 * HB))
                for h in range(HB):
                    act.wait_ge(at_psum, pair_count(p, HB, h + 1))
                    for v in range(2):
                        dst = by_j(a_t[Q * v:Q * v + Q, k, :])[:, h * CB:(h + 1) * CB, :]
                        nc.scalar.copy(dst, bank_chunks(A[h])[Q * k:Q * k + Q, :, :]).then_inc(at_ready, 1)

            def b_hi_part(g, banks=A):
                for h in range(HB):
                    src, dst = b_views(h, banks)
                    act.wait_ge(bt_psum, g * HB + (h + 1))
                    nc.scalar.copy(dst[:, :, 0, :, :], src).then_inc(bt_hi_ready, 1)

            def swap_part(n):
                act.wait_ge(bx_psum, count(n, 1, 1))
                for v in range(2):
                    nc.scalar.copy(swap[Q * v:Q * v + Q, :, :].rearrange("p u t -> p (u t)"),
                                   B[Q - Q * v:P - Q * v, 0:2 * P]).then_inc(swap_ready, 1)

            def x1_hi_part(n):
                for h in range(HB):
                    act.wait_ge(x1_psum, count(n, HB, h + 1))
                    nc.scalar.copy(x1_hi[:, n[1] % 2, h * CB:(h + 1) * CB, :], bank_chunks(X[h])).then_inc(x1_hi_ready, 1)

            def exp_part(t):
                act.wait_ge(gate_step, count(t, GATE, 2))
                nc.scalar.activation(expd[:, :], top[:, 0:1], ACT.Exp, bias=top[:, 1:2],
                                     scale=-1.0).then_inc(exp_ready, 1)

            def out_part(t, part):
                lo, hi = PARTS[part]
                skip = NH if part == 0 else 0
                if part == 0:
                    act.wait_ge(out_stored, count(t, 16, 1))
                act.wait_ge(o_psum, count(t, NP, part + 1))
                nc.scalar.copy(out_sb[:, lo + skip - NH:hi - NH], O[part][:, skip:hi - lo]).then_inc(out_ready[part], 1)

            load_block(0)
            act.dma_start(wr_in[:, :], l1_Wr).then_inc(wr_loaded, 16)
            for m in range(1, 4):
                load_block(m)
            w_hi_part(0)
            load_block(4)
            xt_hi_part(FIRST)
            load_block(5)
            w_hi_part(1)
            w_hi_part(2)
            load_block(6)
            w_hi_part(3)
            a_hi_part(FIRST)
            load_block(7)
            load_block(8)
            load_block(BLOCK_B)
            w_hi_part(4)
            w_hi_part(5)
            b_hi_part(0, SPARE)
            a_part(FIRST, 0)
            w_hi_part(6)
            swap_part((0, 0))
            a_part(FIRST, 1)
            w_hi_part(7)
            x1_hi_part((0, 0))
            w_hi_part(8)
            w_hi_part(9)
            w_hi_part(10)

            def body(t, last_group, last):
                g, i = t
                n = (g, i + 1)
                if not last:
                    xt_hi_part(n)
                    if i % 2 == 1:
                        for k in range(2):
                            a_part((g, i // 2 + 1), k)
                    swap_part(n)
                exp_part(t)
                if i == TPG - 2 and not last_group:
                    b_hi_part(g + 1)
                if not last:
                    x1_hi_part(n)
                out_part(t, 0)
                out_part(t, 1)
                if i % 2 == 0 and not (last_group and i == TPG - 2):
                    a_hi_part((g, i // 2 + 1))
                out_part(t, 2)

            tile_loop(act, body)

        @block.vector
        def _(dve):
            def minus(dst, psum, hi):
                return nc.vector.tensor_tensor(dst, psum, hi.bitcast(F32), ALU.subtract)

            def w_lo_part(k):
                banks = weight_banks(k)
                if k == B_WR:
                    dve.wait_ge(w_hi_ready, HB * k + HB)
                    minus(w_lo[:, :, ER:NH], banks[0][:, 0:C * E].rearrange("p (c e) -> p c e", e=E),
                          w_hi[:, :, ER:NH]).then_inc(w_lo_ready, HB)
                    return
                for h in range(HB):
                    chunks = slice(h * CB, (h + 1) * CB)
                    dst = by_j(lb_lo[:, :])[:, chunks, :] if k == B_LB else w_lo[:, chunks, weight_cols(k)]
                    hi = by_j(lb_hi[:, :])[:, chunks, :] if k == B_LB else w_hi[:, chunks, weight_cols(k)]
                    dve.wait_ge(w_hi_ready, HB * k + h + 1)
                    minus(dst, bank_chunks(banks[h]), hi).then_inc(w_lo_ready, 1)

            def xt_lo_part(n):
                for h in range(HB):
                    chunks = slice(h * CB, (h + 1) * CB)
                    dve.wait_ge(xt_hi_ready, count(n, HB, h + 1))
                    minus(xt[:, chunks, 1, :], bank_chunks(X[h]), xt[:, chunks, 0, :]).then_inc(xt_lo_ready, 1)

            def b_lo_part(g, banks=A):
                for h in range(HB):
                    src, dst = b_views(h, banks)
                    dve.wait_ge(bt_hi_ready, g * HB + (h + 1))
                    minus(dst[:, :, 1, :, :], src, dst[:, :, 0, :, :]).then_inc(bt_ready, 1)

            def bx_part(n, step):
                if step > 0:
                    dve.wait_ge(bx_step, count(n, BX, step))
                if step == 0:
                    dve.wait_ge(swap_ready, count(n, 2, 2))
                    op = nc.vector.tensor_tensor(bx_sum[:, :, :].rearrange("p u t -> p (u t)"), B[:, 0:2 * P],
                                                 swap[:, :, :].rearrange("p u t -> p (u t)"), ALU.add)
                elif step == 1:
                    op = nc.vector.tensor_tensor(bx_all[:, :], bx_sum[:, 0, :], bx_sum[:, 1, :], ALU.add)
                elif step == 2:
                    op = nc.vector.tensor_tensor(bx_own[:, :], bx_all[:, :], own[:, :], ALU.mult)
                elif step == 3:
                    op = nc.vector.tensor_copy(bx_hi[:, :].bitcast(F32R), bx_own[:, :])
                elif step == 4:
                    if n is not FIRST:
                        dve.wait_ge(x1_psum, count(n, HB))
                    op = nc.vector.tensor_copy(bx_t[0:Q, :], bx_own[0:Q, :])
                else:
                    op = nc.vector.tensor_tensor(bx_t[Q:P, :], bx_own[Q:P, :], bx_hi[Q:P, :], ALU.subtract)
                op.then_inc(bx_step, 1)

            def x1_lo_part(n):
                for h in range(HB):
                    dve.wait_ge(x1_hi_ready, count(n, HB, h + 1))
                    src = x1_hi[:, n[1] % 2, h * CB:(h + 1) * CB, :]
                    minus(x1_lo[:, n[1] % 2, h * CB:(h + 1) * CB, :], bank_chunks(X[h]), src).then_inc(x1_lo_ready, 1)

            def gating(t, n, last):
                def after(k):
                    dve.wait_ge(gate_step, count(t, GATE, k))

                def between(step):
                    if not last:
                        bx_part(n, step)

                between(0)
                dve.wait_ge(h_psum, count(t, 1, 1))
                tile_bias = lang_bias[:, bass.ds(count(t, 1), 1), :].rearrange("p a e -> p (a e)")
                nc.vector.tensor_tensor(logit[:, :], O[0][:, ER:NH], tile_bias, ALU.add).then_inc(gate_step, 1)
                after(1)
                between(1)
                nc.vector.max(top[:, :], logit[:, :]).then_inc(gate_step, 1)
                after(2)
                between(2)
                nc.vector.max_index(top_at[:, :], top[:, :], logit[:, :]).then_inc(gate_step, 1)
                between(3)
                between(4)
                after(3)
                nc.vector.tensor_copy(top_no[:, :], top_at[:, 0:2]).then_inc(gate_step, 1)
                dve.wait_ge(exp_ready, count(t, 1, 1))
                nc.vector.tensor_scalar(half_sum[:, :], expd[:, :], 1.0, 0.5, ALU.add, ALU.mult).then_inc(gate_step, 1)
                between(5)
                after(5)
                nc.vector.reciprocal(weight[:, 0:1], half_sum[:, :]).then_inc(gate_step, 1)
                after(6)
                nc.vector.tensor_tensor(weight[:, 1:2], weight[:, 0:1], expd[:, :], ALU.mult).then_inc(gate_step, 1)
                nc.vector.tensor_scalar(gate1[:, :], expert_no[:, :], top_no[:, 0:1], weight[:, 0:1],
                                        ALU.is_equal, ALU.mult).then_inc(gate_step, 1)
                after(7)
                nc.vector.tensor_scalar(gate2[:, :], expert_no[:, :], top_no[:, 1:2], weight[:, 1:2],
                                        ALU.is_equal, ALU.mult).then_inc(gate_step, 1)
                after(9)
                nc.vector.tensor_tensor(gate[:, :], gate1[:, :], gate2[:, :], ALU.add).then_inc(gate_step, 1)
                after(10)
                nc.vector.tensor_tensor(gated[:, :, :], O[0][:, 0:ER].rearrange("p (e r) -> p e r", r=R),
                                        gate[:, :].unsqueeze(2).to_broadcast([P, E, R]),
                                        ALU.mult).then_inc(gate_step, 1)

            def gated_t_part(t):
                dve.wait_ge(gt_psum, count(t, 1, 1))
                nc.vector.tensor_copy(gt_hi[:, :], B[:, 2 * P:3 * P]).then_inc(gt_ready, 1)
                dve.wait_ge(gt_ready, count(t, 2, 1))
                minus(gt_lo[:, :], B[:, 2 * P:3 * P], gt_hi[:, :]).then_inc(gt_ready, 1)

            dve.wait_ge(consts_set, E + 1 + BPT)
            dve.wait_ge(own_psum, 1)
            nc.vector.tensor_copy(own[:, :], B[:, 0:P]).then_inc(own_ready, 1)
            dve.wait_ge(lid_in, 16)
            for b in range(BPT):
                nc.vector.tensor_copy(lidf[S * b:S * b + S, :],
                                      lid[S * b:S * b + S, :].rearrange("p (t b) -> p t b", b=BPT)[:, :, b])\
                    .then_inc(lid_ready, 1)
            dve.wait_ge(lid_ready, BPT)
            nc.vector.tensor_tensor(lang_bias[:, :, :], lidf[:, :].unsqueeze(2).to_broadcast([P, T, E]),
                                    expert_no[:, :].unsqueeze(1).to_broadcast([P, T, E]),
                                    ALU.is_equal).then_inc(lid_ready, 1)
            dve.wait_ge(lid_ready, BPT + 1)
            nc.vector.tensor_scalar(lang_bias[:, :, :], lang_bias[:, :, :], LANG_BIAS, None,
                                    ALU.mult).then_inc(tables_set, 1)
            dve.wait_ge(tables_set, 1)
            dve.wait_ge(own_ready, 1)
            w_lo_part(0)
            xt_lo_part((0, 0))
            for k in range(1, 6):
                w_lo_part(k)
            b_lo_part(0, SPARE)
            w_lo_part(6)
            for step in range(BX):
                bx_part(FIRST, step)
            w_lo_part(7)
            x1_lo_part((0, 0))
            w_lo_part(8)
            w_lo_part(9)
            w_lo_part(10)

            def body(t, last_group, last):
                g, i = t
                n = (g, i + 1)
                if not last:
                    xt_lo_part(n)
                gating(t, n, last)
                if i == TPG - 2 and not last_group:
                    b_lo_part(g + 1)
                    gated_t_part(t)
                    x1_lo_part(n)
                else:
                    if not last:
                        x1_lo_part(n)
                    gated_t_part(t)

            tile_loop(dve, body)


_INS = ["x", "itok_B_4_50", "itok_B_0_7", "L0_cond_A", "L0_cond_B", "L1_cond_W", "L1_cond_Wr", "L1_cond_A", "L1_cond_B"]


def kernel(**inputs):
    import numpy as _np
    import concourse.bacc as _bacc
    from concourse import mybir as _mybir
    from concourse.bass_utils import run_bass_kernel_spmd as _run

    nc = _bacc.Bacc("TRN2", target_bir_lowering=False, num_devices=1)
    arrays, args = {}, []
    for name in _INS:
        a = _np.ascontiguousarray(inputs[name])
        arrays[f"in_{name}_dram"] = a
        args.append(nc.dram_tensor(f"in_{name}_dram", a.shape, _mybir.dt.from_np(a.dtype), kind="ExternalInput").ap())
    shape = inputs["x"].shape
    args.append(nc.dram_tensor("out_0_dram", shape, _mybir.dt.float32, kind="ExternalOutput").ap())
    two_adapter_layers(nc, *args)
    r = _run(nc, [arrays], core_ids=[0])
    return r.results[0]["out_0_dram"]
```
